# Optimizing a Trainium2 kernel written in Bass

```python
import numpy as np
import jax
import jax.numpy as jnp

def _softmax(x, axis=-1):
    return jax.nn.softmax(x, axis=axis)

def _gelu(x):
    return jax.nn.gelu(x, approximate=True)

def _silu(x):
    return jax.nn.silu(x)

def _sigmoid(x):
    return jax.nn.sigmoid(x)

def _layernorm(x, axis=-1, eps=1e-05):
    m = jnp.mean(x, axis=axis, keepdims=True)
    v = jnp.var(x, axis=axis, keepdims=True)
    return (x - m) / jnp.sqrt(v + eps)

def _scatter_add(tgt, idx, src, axis=0):
    return tgt.at[idx].add(src)

def _segment_sum(src, seg, n):
    return jax.ops.segment_sum(src, seg, n)
kernel_name = 'mk_decoder_postln_d1_seqx_r4_8337d4'

def setup_inputs(seed: int=0):
    np.random.seed(seed)
    _w = jnp.asarray

    def _rec_inputs():
        import jax
        import jax.numpy as jnp
        _rk = jax.random.key(seed)
        x = 7.22e-05 + 1 * jax.random.normal(jax.random.fold_in(_rk, 1), (16, 256, 256), jnp.float32)
        _lenS = 256 - jax.random.randint(jax.random.fold_in(_rk, 7), (16,), 0, max(1, 256 // 4) + 1, jnp.int32)
        _lenS2 = 256 - jax.random.randint(jax.random.fold_in(_rk, 8), (16,), 0, max(1, 256 // 4) + 1, jnp.int32)
        _ctx_1024P = jax.random.normal(jax.random.fold_in(_rk, 11), (16, 16, 256), jnp.float32)
        _ctx_1024c = jax.random.dirichlet(jax.random.fold_in(_rk, 511), 0.3 * jnp.ones((16,), jnp.float32), (16, 256))
        _ctx_1024t = jnp.einsum('bsk,bkd->bsd', _ctx_1024c, _ctx_1024P)
        _ctx_1024t = _ctx_1024t * jax.lax.rsqrt(jnp.mean(jnp.square(_ctx_1024t)) + 1e-12) * 0.953939
        ctx_1024 = 4.13588e-05 + 0.999923 * (_ctx_1024t + 0.3 * jax.random.normal(jax.random.fold_in(_rk, 611), (16, 256, 256), jnp.float32))
        return (x, ctx_1024)
    x, ctx_1024 = _rec_inputs()

    def _L0_attn_setup():
        import jax, jax.numpy as jnp
        import numpy as np
        EMB = 256
        HEADS = 16
        HEADSIZE = EMB // HEADS
        EPS = 1e-05

        def _layernorm(x, g, b):
            m = jnp.mean(x, axis=-1, keepdims=True)
            v = jnp.mean((x - m) ** 2, axis=-1, keepdims=True)
            return (x - m) * jax.lax.rsqrt(v + EPS) * g + b
        key = jax.random.key(seed)
        ks = jax.random.split(key, 6)
        B, T = (4, 512)
        s = 1.0 / np.sqrt(EMB)
        return {'x': jax.random.normal(ks[0], (B, T, EMB), dtype=jnp.float32), 'Wk': jax.random.normal(ks[1], (EMB, EMB), dtype=jnp.float32) * s, 'Wq': jax.random.normal(ks[2], (EMB, EMB), dtype=jnp.float32) * s, 'Wv': jax.random.normal(ks[3], (EMB, EMB), dtype=jnp.float32) * s, 'Wo': jax.random.normal(ks[4], (EMB, EMB), dtype=jnp.float32) * s, 'bo': jnp.zeros((EMB,), dtype=jnp.float32), 'kln_g': jnp.ones((HEADSIZE,), dtype=jnp.float32), 'kln_b': jnp.zeros((HEADSIZE,), dtype=jnp.float32), 'qln_g': jnp.ones((HEADSIZE,), dtype=jnp.float32), 'qln_b': jnp.zeros((HEADSIZE,), dtype=jnp.float32)}
    _L0_attn_all = _L0_attn_setup()
    _L0_attn_in = {k: v for k, v in _L0_attn_all.items() if k in ('Wk', 'Wq', 'Wv', 'Wo', 'bo', 'kln_g', 'kln_b', 'qln_g', 'qln_b')}
    del _L0_attn_all

    def _L0_xattn_setup():
        import jax, jax.numpy as jnp
        import numpy as np
        D_MODEL = 256
        NUM_HEADS = 16
        HEAD_DIM = D_MODEL // NUM_HEADS
        ROPE_BASE = 10000.0

        def _rope_cos_sin(seq_len, head_dim, dtype):
            inv_freq = 1.0 / ROPE_BASE ** (jnp.arange(0, head_dim, 2, dtype=jnp.float32) / head_dim)
            t = jnp.arange(seq_len, dtype=jnp.float32)
            freqs = jnp.einsum('i,j->ij', t, inv_freq)
            emb = jnp.concatenate([freqs, freqs], axis=-1)
            return (jnp.cos(emb).astype(dtype), jnp.sin(emb).astype(dtype))

        def _rotate_half(x):
            x1, x2 = jnp.split(x, 2, axis=-1)
            return jnp.concatenate([-x2, x1], axis=-1)
        key = jax.random.key(seed)
        ks = jax.random.split(key, 12)
        B, S, D = (4, 512, D_MODEL)
        scale = 1.0 / np.sqrt(D)
        inp = {'query': jax.random.normal(ks[0], (B, S, D), jnp.float32), 'key': jax.random.normal(ks[1], (B, S, D), jnp.float32), 'value': jax.random.normal(ks[2], (B, S, D), jnp.float32), 'Wq': jax.random.normal(ks[3], (D, D), jnp.float32) * scale, 'bq': jnp.zeros((D,), jnp.float32), 'Wk': jax.random.normal(ks[4], (D, D), jnp.float32) * scale, 'bk': jnp.zeros((D,), jnp.float32), 'Wv': jax.random.normal(ks[5], (D, D), jnp.float32) * scale, 'bv': jnp.zeros((D,), jnp.float32), 'Wo': jax.random.normal(ks[6], (D, D), jnp.float32) * scale, 'bo': jnp.zeros((D,), jnp.float32)}
        return inp
    _L0_xattn_all = _L0_xattn_setup()
    _L0_xattn_in = {k: v for k, v in _L0_xattn_all.items() if k in ('Wq', 'bq', 'Wk', 'bk', 'Wv', 'bv', 'Wo', 'bo')}
    del _L0_xattn_all

    def _L0_ffn_setup():
        import jax, jax.numpy as jnp
        import numpy as np
        S, B, H, F, E, K = (512, 2, 256, 512, 8, 2)

        def _moe_forward(hidden_states, router_w, w1, b1, w2, b2):
            s, b, h = hidden_states.shape
            T = s * b
            x = hidden_states.reshape(T, h)
            logits = jnp.einsum('th,eh->te', x, router_w)
            topk_logits, topk_idx = jax.lax.top_k(logits, K)
            probs = jax.nn.softmax(topk_logits, axis=-1)
            combine = jnp.zeros((T, E), dtype=x.dtype)
            combine = combine.at[jnp.arange(T)[:, None], topk_idx].add(probs.astype(x.dtype))
            hmid = jnp.einsum('th,efh->etf', x, w1) + b1[:, None, :]
            hmid = jax.nn.gelu(hmid, approximate=False)
            y = jnp.einsum('etf,ehf->eth', hmid, w2) + b2[:, None, :]
            out = jnp.einsum('eth,te->th', y, combine)
            return out.reshape(s, b, h)
        key = jax.random.key(seed)
        ks = jax.random.split(key, 6)
        std = 0.02
        return {'hidden_states': jax.random.normal(ks[0], (S, B, H), dtype=jnp.float32), 'router_w': jax.random.normal(ks[1], (E, H), dtype=jnp.float32) * std, 'w1': jax.random.normal(ks[2], (E, F, H), dtype=jnp.float32) * (1.0 / np.sqrt(H)), 'b1': jnp.zeros((E, F), dtype=jnp.float32), 'w2': jax.random.normal(ks[3], (E, H, F), dtype=jnp.float32) * (1.0 / np.sqrt(F)), 'b2': jnp.zeros((E, H), dtype=jnp.float32)}
    _L0_ffn_all = _L0_ffn_setup()
    _L0_ffn_in = {k: v for k, v in _L0_ffn_all.items() if k in ('router_w', 'w1', 'b1', 'w2', 'b2')}
    del _L0_ffn_all
    return {'x': x, 'ctx_1024': ctx_1024, 'L0_attn_Wk': _L0_attn_in['Wk'], 'L0_attn_Wq': _L0_attn_in['Wq'], 'L0_attn_Wv': _L0_attn_in['Wv'], 'L0_attn_Wo': _L0_attn_in['Wo'], 'L0_attn_bo': _L0_attn_in['bo'], 'L0_attn_kln_g': _L0_attn_in['kln_g'], 'L0_attn_kln_b': _L0_attn_in['kln_b'], 'L0_attn_qln_g': _L0_attn_in['qln_g'], 'L0_attn_qln_b': _L0_attn_in['qln_b'], 'L0_xattn_Wq': _L0_xattn_in['Wq'], 'L0_xattn_bq': _L0_xattn_in['bq'], 'L0_xattn_Wk': _L0_xattn_in['Wk'], 'L0_xattn_bk': _L0_xattn_in['bk'], 'L0_xattn_Wv': _L0_xattn_in['Wv'], 'L0_xattn_bv': _L0_xattn_in['bv'], 'L0_xattn_Wo': _L0_xattn_in['Wo'], 'L0_xattn_bo': _L0_xattn_in['bo'], 'L0_ffn_router_w': _L0_ffn_in['router_w'], 'L0_ffn_w1': _L0_ffn_in['w1'], 'L0_ffn_b1': _L0_ffn_in['b1'], 'L0_ffn_w2': _L0_ffn_in['w2'], 'L0_ffn_b2': _L0_ffn_in['b2']}

def reference(x, ctx_1024, L0_attn_Wk, L0_attn_Wq, L0_attn_Wv, L0_attn_Wo, L0_attn_bo, L0_attn_kln_g, L0_attn_kln_b, L0_attn_qln_g, L0_attn_qln_b, L0_xattn_Wq, L0_xattn_bq, L0_xattn_Wk, L0_xattn_bk, L0_xattn_Wv, L0_xattn_bv, L0_xattn_Wo, L0_xattn_bo, L0_ffn_router_w, L0_ffn_w1, L0_ffn_b1, L0_ffn_w2, L0_ffn_b2):
    import jax
    import jax.numpy as jnp

    def _L0_attn_ref(x, Wk, Wq, Wv, Wo, bo, kln_g, kln_b, qln_g, qln_b):
        import jax, jax.numpy as jnp
        import numpy as np
        EMB = 256
        HEADS = 16
        HEADSIZE = EMB // HEADS
        EPS = 1e-05

        def _layernorm(x, g, b):
            m = jnp.mean(x, axis=-1, keepdims=True)
            v = jnp.mean((x - m) ** 2, axis=-1, keepdims=True)
            return (x - m) * jax.lax.rsqrt(v + EPS) * g + b
        B, T, E = x.shape
        k = jnp.einsum('bte,fe->btf', x, Wk).reshape(B, T, HEADS, HEADSIZE)
        q = jnp.einsum('bte,fe->btf', x, Wq).reshape(B, T, HEADS, HEADSIZE)
        v = jnp.einsum('bte,fe->btf', x, Wv).reshape(B, T, HEADS, HEADSIZE)
        k = _layernorm(k, kln_g, kln_b)
        q = _layernorm(q, qln_g, qln_b)
        scale = E ** (-0.25)
        q = q * scale
        k = k * scale
        dot = jnp.einsum('bihd,bjhd->bhij', q, k)
        causal = jnp.triu(jnp.ones((T, T), dtype=bool), k=1)
        dot = jnp.where(causal, -jnp.inf, dot)
        att = jax.nn.softmax(dot, axis=-1)
        out = jnp.einsum('bhij,bjhd->bihd', att, v).reshape(B, T, E)
        return jnp.einsum('bte,fe->btf', out, Wo) + bo

    def _L0_xattn_ref(query, key, value, Wq, bq, Wk, bk, Wv, bv, Wo, bo):
        import jax, jax.numpy as jnp
        import numpy as np
        D_MODEL = 256
        NUM_HEADS = 16
        HEAD_DIM = D_MODEL // NUM_HEADS
        ROPE_BASE = 10000.0

        def _rope_cos_sin(seq_len, head_dim, dtype):
            inv_freq = 1.0 / ROPE_BASE ** (jnp.arange(0, head_dim, 2, dtype=jnp.float32) / head_dim)
            t = jnp.arange(seq_len, dtype=jnp.float32)
            freqs = jnp.einsum('i,j->ij', t, inv_freq)
            emb = jnp.concatenate([freqs, freqs], axis=-1)
            return (jnp.cos(emb).astype(dtype), jnp.sin(emb).astype(dtype))

        def _rotate_half(x):
            x1, x2 = jnp.split(x, 2, axis=-1)
            return jnp.concatenate([-x2, x1], axis=-1)
        B, T, D = query.shape
        H, hd = (NUM_HEADS, HEAD_DIM)
        Q = (query @ Wq + bq).reshape(B, T, H, hd).transpose(0, 2, 1, 3)
        K = (key @ Wk + bk).reshape(B, -1, H, hd).transpose(0, 2, 1, 3)
        V = (value @ Wv + bv).reshape(B, -1, H, hd).transpose(0, 2, 1, 3)
        cos, sin = _rope_cos_sin(T, hd, Q.dtype)
        Q = Q * cos + _rotate_half(Q) * sin
        K = K * cos + _rotate_half(K) * sin
        scores = jnp.einsum('bhtd,bhsd->bhts', Q, K) / jnp.sqrt(jnp.asarray(hd, Q.dtype))
        attn = jax.nn.softmax(scores, axis=-1)
        context = jnp.einsum('bhts,bhsd->bhtd', attn, V)
        context = context.transpose(0, 2, 1, 3).reshape(B, T, D)
        return context @ Wo + bo

    def _L0_ffn_ref(hidden_states, router_w, w1, b1, w2, b2):
        import jax, jax.numpy as jnp
        import numpy as np
        S, B, H, F, E, K = (512, 2, 256, 512, 8, 2)

        def _moe_forward(hidden_states, router_w, w1, b1, w2, b2):
            s, b, h = hidden_states.shape
            T = s * b
            x = hidden_states.reshape(T, h)
            logits = jnp.einsum('th,eh->te', x, router_w)
            topk_logits, topk_idx = jax.lax.top_k(logits, K)
            probs = jax.nn.softmax(topk_logits, axis=-1)
            combine = jnp.zeros((T, E), dtype=x.dtype)
            combine = combine.at[jnp.arange(T)[:, None], topk_idx].add(probs.astype(x.dtype))
            hmid = jnp.einsum('th,efh->etf', x, w1) + b1[:, None, :]
            hmid = jax.nn.gelu(hmid, approximate=False)
            y = jnp.einsum('etf,ehf->eth', hmid, w2) + b2[:, None, :]
            out = jnp.einsum('eth,te->th', y, combine)
            return out.reshape(s, b, h)
        return _moe_forward(hidden_states, router_w, w1, b1, w2, b2)
    x = _layernorm(x + _L0_attn_ref(x, L0_attn_Wk, L0_attn_Wq, L0_attn_Wv, L0_attn_Wo, L0_attn_bo, L0_attn_kln_g, L0_attn_kln_b, L0_attn_qln_g, L0_attn_qln_b), axis=-1)
    x = _layernorm(x + _L0_xattn_ref(x, ctx_1024, ctx_1024, L0_xattn_Wq, L0_xattn_bq, L0_xattn_Wk, L0_xattn_bk, L0_xattn_Wv, L0_xattn_bv, L0_xattn_Wo, L0_xattn_bo), axis=-1)
    x = _layernorm(x + _L0_ffn_ref(x, L0_ffn_router_w, L0_ffn_w1, L0_ffn_b1, L0_ffn_w2, L0_ffn_b2), axis=-1)
    return x

_drawn_inputs = setup_inputs


def setup_inputs(seed=0):
    import zlib

    import numpy as np

    out = dict(_drawn_inputs(seed))
    spreads = {'L0_attn_bo': (0.0, 0.1),
     'L0_attn_kln_g': (1.0, 0.2),
     'L0_attn_kln_b': (0.0, 0.8),
     'L0_attn_qln_g': (1.0, 0.2),
     'L0_attn_qln_b': (0.0, 0.316),
     'L0_xattn_bq': (0.0, 0.1),
     'L0_xattn_bk': (0.0, 0.1),
     'L0_xattn_bv': (0.0, 0.1),
     'L0_xattn_bo': (0.0, 0.1),
     'L0_ffn_b1': (0.0, 0.1),
     'L0_ffn_b2': (0.0, 0.1)}
    factors = {}
    for name, (base, spread) in spreads.items():
        noise = np.random.default_rng([zlib.crc32(name.encode()), seed]).standard_normal(out[name].shape)
        drawn = base * np.exp(spread * noise) if base else spread * noise
        out[name] = jnp.asarray(drawn.astype(out[name].dtype))
    for name, factor in factors.items():
        out[name] = (out[name] * factor).astype(out[name].dtype)
    return out
```

```python
from contextlib import ExitStack

import numpy as np

import concourse.bass as bass
from concourse import mybir

F32 = mybir.dt.float32
BF16 = mybir.dt.bfloat16
I32 = mybir.dt.int32
U32 = mybir.dt.uint32
ALU = mybir.AluOpType
ACT = mybir.ActivationFunctionType
AX = mybir.AxisListType

P = 128
B, T, E, H = 16, 256, 256, 16
D = E // H
NT = T // P
KC = E // P
N = B * T
NE, F, TOPK = 8, 512, 2
FC = F // P
EPS = 1e-5
GRP = 4
NG = H // GRP
NU = NG * NT
SLOTS = ((0, 0), (0, 1), (1, 0), (1, 1), (0, 2), (2, 0))
ROWS = len(SLOTS) * D
MASKED = -1e30
MAGIC = 0x5F3759DF - 2 ** 31

REGION = N + P
PADS = NE * REGION
ROW = 272
COL_CW, COL_ID = E, E + NE
TILES = (TOPK * N + NE * (P - 1)) // P + 1
TILES += TILES % 2
N_CST = 18
N_READY = 12
LNB = 4


class Signal:

    def __init__(self, sem, n, first=0):
        self.sem, self.n, self.first = sem, n, first

    def after(self, b, k=None):
        return (b - self.first) * self.n + (self.n if k is None else k)

    def begun(self, b, k=None):
        v = self.after(b, k)
        return not isinstance(v, int) or v > 0

    def counter(self, b):
        k = [0]

        def count():
            k[0] += 1
            return self.after(b, k[0])
        return count


class Paired:

    def __init__(self, sems, n):
        self.sems, self.n = sems, n

    def after(self, b, p):
        return (b - p) * (self.n // 2) + self.n


def rsqrt_steps(dve, sem, count, v, hv, y, t0, t1):
    dve.tensor_scalar(t0.bitcast(I32), v.bitcast(I32), 1, None, ALU.logical_shift_right).then_inc(sem, 1)
    dve.wait_ge(sem, count())
    dve.tensor_scalar(y.bitcast(I32), t0.bitcast(I32), -1.0, float(MAGIC), ALU.mult, ALU.add).then_inc(sem, 1)
    dve.wait_ge(sem, count())
    for _ in range(3):
        dve.tensor_tensor(t0, y, y, ALU.mult).then_inc(sem, 1)
        dve.wait_ge(sem, count())
        dve.tensor_tensor(t1, t0, hv, ALU.mult).then_inc(sem, 1)
        dve.wait_ge(sem, count())
        dve.scalar_tensor_tensor(out=y, in0=t1, scalar=1.5, in1=y, op0=ALU.subtract, op1=ALU.mult
                                 ).then_inc(sem, 1)
        dve.wait_ge(sem, count())


def decoder_block(nc, x, xT, ctxT, wqk_self, wv_self, wo_self, wq_x, wk_x, wv_x, wo_x, bo_self, bo_x,
                  gains, shifts, bq_x, bk_x, bv_x, rope, router, w1, b1, w2, b2, consts, tables, out):
    x1_dram = nc.dram_tensor("x1_dram", (N, E), F32, kind="Internal").ap()
    acc_dram = nc.dram_tensor("acc_dram", (N + P, E), F32, kind="Internal").ap()
    xs_dram = nc.dram_tensor("xs_dram", (PADS + P, ROW), F32, kind="Internal").ap()
    part_dram = nc.dram_tensor("part_dram", (2, 3, 2, E, T), BF16, kind="Internal").ap()

    with ExitStack() as ctx:
        def sb(name, shape, dt=F32):
            return ctx.enter_context(nc.sbuf_tensor(name, shape, dt))

        def sem(name):
            return ctx.enter_context(nc.semaphore(name))

        def signal(name, n, first=0):
            return Signal(sem(name), n, first)

        def paired(name, n):
            return Paired([sem(f"{name}_{p}") for p in range(2)], n)

        def apart(eng):
            eng.sem_inc(passed, 1)

        ident = sb("ident", [P, P])
        identb = sb("identb", [P, P], BF16)
        maskb = sb("maskb", [P, P], BF16)
        trib = sb("trib", [P, P], BF16)
        onesb = sb("onesb", [P, P], BF16)
        cst = sb("cst", [P, 3, P])
        small = sb("small", [P, 256])
        w_qk = sb("w_qk", [P, KC, 2 * E])
        w_v = sb("w_v", [P, KC, E])
        w_o = sb("w_o", [P, KC, E])
        wx_q = sb("wx_q", [P, KC, E])
        wx_k = sb("wx_k", [P, KC, E])
        wx_v = sb("wx_v", [P, KC, E])
        wx_o = sb("wx_o", [P, KC, E])
        bo = sb("bo", [P, 2, E])
        bqk = sb("bqk", [P, 2, E])
        bv = sb("bv", [P, E])
        gb = sb("gb", [P, 2, NT, 2, D])
        cs = sb("cs", [P, 2, NT, 2, D])
        rw = sb("rw", [P, KC, NE])
        w1s = sb("w1s", [P, KC, NE, F])
        w2s = sb("w2s", [P, FC, NE, E])
        mix = sb("mix", [P, NE * F])
        b1s = mix[:].rearrange("p (e f) -> p e f", e=NE)

        xin = sb("xin", [P, 2, KC, T])
        xnat = sb("xnat", [P, 2, NT, E])
        xb = sb("xb", [P, 2, NT, E])
        x1T = sb("x1T", [P, KC, T])
        qkn = sb("qkn", [P, NT, 2 * E])
        xc = sb("xc", [P, NT, 2 * E])
        sq = sb("sq", [P, NT, 2 * E])
        st = sb("st", [P, 6, 64])
        th = sb("th", [P, 3, 4, T], BF16)
        rr = sb("rr", [P, NT, 4, P])
        qst = sb("qst", [ROWS + 1, 2, H, T], BF16)
        kst = sb("kst", [ROWS + 1, 2, H, T], BF16)
        vaug = mix[:, 0:2048].rearrange("p (a t h d) -> p a t h d", a=2, t=NT, h=H)
        nmax = sb("nmax", [P, NT, H])
        nmaxT = sb("nmaxT", [H, T], BF16)
        pT = sb("pT", [P, 3, GRP, T])
        b2s = pT[:].rearrange("p u h t -> p (u h t)")[:, 0:NE * E].rearrange("p (e f) -> p e f", e=NE)
        oT = mix[:, 2048:3072].rearrange("p (g t) -> p g t", g=NG)
        rec = sb("rec", [P, NT, H])
        on = mix[:, 3072:3584].rearrange("p (t e) -> p t e", t=NT)
        onT = mix[:, 3584:4096].rearrange("p (c t) -> p c t", c=KC)
        y = sb("y", [P, NT, E])
        bst = sb("bst", [P, LNB, 6])
        mv = sb("mv", [P, LNB, 2])
        ls = sb("ls", [P, 5, LNB])
        xo = sb("xo", [P, NT, E])

        pay = sb("pay", [P, NT, ROW])
        x2T = sb("x2T", [P, KC, T])
        lg = sb("lg", [P, NT, NE])
        mx8 = sb("mx8", [P, NT, 8])
        ix8 = sb("ix8", [P, NT, 8], U32)
        ixf = sb("ixf", [P, NT, TOPK])
        oh = sb("oh", [P, NT, TOPK, NE])
        ohb = sb("ohb", [P, NT, NE], BF16)
        rank = sb("rank", [P, NT, NE])
        carry = sb("carry", [P, NE])
        sel = sb("sel", [P, NT, TOPK, NE])
        posf = sb("posf", [P, NT * TOPK])
        posi = sb("posi", [P, NT * TOPK], I32)
        prob = sb("prob", [P, NT, TOPK])
        pe1 = sb("pe1", [P, 3, NT])
        idf = sb("idf", [P, NT])

        cnt = sb("cnt", [P, 8, NE])
        cnti = sb("cnti", [P, 2, NE], I32)
        tbl = sb("tbl", [P, 2, TILES])
        tbli = sb("tbli", [P, 2, TILES], I32)
        rows = sb("rows", [P, 2, ROW])
        rowid = sb("rowid", [P, 2, 1], I32)
        meta = sb("meta", [P, 2, NE + 1])
        ye = sb("ye", [P, 2, E])
        xsT = xin[:].rearrange("p a c t -> p a (c t)")[:, :, 0:E]
        hpre = xnat[:].rearrange("p a t e -> p a (t e)")
        hact = xb[:].rearrange("p a t e -> p a (t e)")
        hT = qkn[:]
        lnx = w1s[:].rearrange("p c e f -> p (c e f)")[:, 0:2 * LNB * E].rearrange(
            "p (a n e) -> p a n e", a=2, n=LNB)

        PS = ctx.enter_context(nc.psum_tensor("PS", [P, 4096], F32))
        S = [PS[:, 0:1024], PS[:, 1024:2048]]
        O = PS[:, 2048:3072]
        M0, M1 = PS[:, 3072:3584], PS[:, 3584:4096]

        cst_in = sem("cst_in")
        passed = sem("passed")
        cst_ready = sem("cst_ready")
        moe_in = sem("moe_in")
        xin_in = paired("xin_in", 16)
        xnat_in = paired("xnat_in", 16)
        xb_ready = signal("xb_ready", 1)
        x1T_pe, x1T_ready = signal("x1T_pe", 1, B), signal("x1T_ready", 1, B)
        v_pe, v_ready = signal("v_pe", 1), signal("v_ready", 1)
        qk_pe, qk_ready = signal("qk_pe", NT), signal("qk_ready", NT)
        norm_link = signal("norm_link", 16)
        centered, squared = signal("centered", 1), signal("squared", 1)
        gain_link = signal("gain_link", 2)
        cosined = signal("cosined", 1, B)
        rope_link = signal("rope_link", 3, B)
        turned = signal("turned", NT)
        hi_ready, rest_ready = signal("hi_ready", NT), signal("rest_ready", NT)
        mid_ready, lo_ready = signal("mid_ready", NT), signal("lo_ready", NT)
        parts_out = signal("parts_out", 16)
        stack_in = signal("stack_in", 16 * 2 * len(SLOTS))
        scores_pe, max_ready = signal("scores_pe", NU), signal("max_ready", NU)
        maxT_pe, maxT_ready = signal("maxT_pe", 1), signal("maxT_ready", 1)
        max_in = signal("max_in", 16)
        scoresT_pe, exp_ready = signal("scoresT_pe", NU), signal("exp_ready", NU)
        masked = signal("masked", NU)
        pv_pe = signal("pv_pe", NU)
        oT_a, oT_b = signal("oT_a", 1), signal("oT_b", 1)
        o_pe = signal("o_pe", NT)
        rec_ready, on_ready = signal("rec_ready", NT), signal("on_ready", NT)
        onT_pe, onT_ready = signal("onT_pe", 1), signal("onT_ready", 1)
        wo_pe = signal("wo_pe", 1)
        y_link = signal("y_link", 5 + 2 + 11)
        xo_ready = signal("xo_ready", NT)
        x1_out, x2_out = signal("x1_out", 16), signal("x2_out", 16, B)
        x2T_pe, x2T_ready = signal("x2T_pe", 1, B), signal("x2T_ready", 1, B)
        logits_pe = signal("logits_pe", 1, B)
        router_link = signal("router_link", 18, B)
        gap_ready, e_ready = signal("gap_ready", 1, B), signal("e_ready", 1, B)
        hot_ready, rank_pe = signal("hot_ready", 1, B), signal("rank_pe", 1, B)
        rank_ready = signal("rank_ready", 1, B)
        row_ready = signal("row_ready", 1, B)
        scattered = signal("scattered", 16 * NT * TOPK, B)

        biases_in = sem("biases_in")
        table_link = signal("table_link", 20)
        table_ready = sem("table_ready")
        pads_out = sem("pads_out")
        pads_scattered = sem("pads_scattered")
        rows_in = paired("rows_in", 16)
        meta_ready = signal("meta_ready", 1)
        xsT_pe, xsT_ready = signal("xsT_pe", 1), signal("xsT_ready", 1)
        h_pe, hpre_ready, hact_ready = signal("h_pe", 1), signal("hpre_ready", 1), signal("hact_ready", 1)
        hT_pe, hT_ready = signal("hT_pe", 1), signal("hT_ready", 1)
        y_pe, ye_link = signal("y_pe", 1), signal("ye_link", 3)
        added = signal("added", 16)
        ln_in, ln_out = paired("ln_in", 16), signal("ln_out", 16)
        ln_link, ln_ready = signal("ln_link", 2 * LNB + 2 + 11), signal("ln_ready", LNB)

        iota8 = small[:, 0:8]
        iota8_region = small[:, 8:16]
        pcol = small[:, 16:17]
        idcol = small[:, 17:18]
        jrow = small[:, 32:32 + TILES]
        tri8 = small[:, 128:192].rearrange("p (e f) -> p e f", e=NE)
        assert 32 + TILES <= 128

        def groups16(ap):
            return ap[:].rearrange("p t (h d) -> p (t h) d", d=D)

        def bc(ap, n):
            return ap.unsqueeze(len(ap.shape)).to_broadcast(list(ap.shape) + [n])

        def heads4(ap):
            return ap[:].rearrange("p t (q h d) -> p (t q) h d", q=2, d=D)

        def per_head(table):
            a = table.rearrange("p t q d -> p (t q) d").unsqueeze(2)
            return a.to_broadcast([P, NT * 2, H, table.shape[3]])

        def keys_of(cross, t):
            return T if cross else (t + 1) * P

        def queries_of(cross, kt):
            return 0 if cross else kt * P

        TURN_AT = 5

        def routes_last(b, cross):
            return cross and not (isinstance(b, int) and b == B)

        def over(step, in_loop_pairs):
            step(0, False, None, False, 0)
            step(1, False, 0, False, 1)
            step(2, False, 1, False, 0)
            with in_loop_pairs(1, B // 2 - 1) as j:
                step(2 * j + 1, False, 2 * j, False, 1)
                step(2 * j + 2, False, 2 * j + 1, False, 0)
            step(B - 1, False, B - 2, False, 1)
            step(B, True, B - 1, False, 0)
            step(B + 1, True, B, True, 1)
            step(B + 2, True, B + 1, True, 0)
            with in_loop_pairs(B // 2 + 1, B - 1) as j:
                step(2 * j + 1, True, 2 * j, True, 1)
                step(2 * j + 2, True, 2 * j + 1, True, 0)
            step(2 * B - 1, True, 2 * B - 2, True, 1)
            step(None, True, 2 * B - 1, True, 0)

        def over_tiles(step, loop):
            step(0, None, 0)
            step(1, 0, 1)
            step(2, 1, 0)
            with loop(1, TILES // 2 - 1) as i:
                step(2 * i + 1, 2 * i, 1)
                step(2 * i + 2, 2 * i + 1, 0)
            step(TILES - 1, TILES - 2, 1)
            step(None, TILES - 1, 0)

        def over_ln(step, loop):
            step(0, 0)
            step(1, 1)
            with loop(1, N // P // LNB // 2) as i:
                step(2 * i, 0)
                step(2 * i + 1, 1)

        def expert_of(eng, j):
            return eng.value_load(tbli[0:1, 0, bass.ds(j, 1)], min_val=0, max_val=NE - 1)

        block = ctx.enter_context(nc.Block())

        @block.sync
        def _(sp):
            def load(b, cross, p):
                if v_pe.begun(b - 2):
                    sp.wait_ge(v_pe.sem, v_pe.after(b - 2))
                if qk_pe.begun(b - 2):
                    sp.wait_ge(qk_pe.sem, qk_pe.after(b - 2))
                src = (ctxT if cross else xT).rearrange("(c p) n -> p c n", p=P)
                s = b - B if cross else b
                apart(sp)
                sp.dma_start(xin[:, p], src[:, :, bass.ds(s * T, T)]).then_inc(xin_in.sems[p], 16)
                if xb_ready.begun(b - 2):
                    sp.wait_ge(xb_ready.sem, xb_ready.after(b - 2))
                apart(sp)
                if cross:
                    if x1T_pe.begun(b - 2):
                        sp.wait_ge(x1T_pe.sem, x1T_pe.after(b - 2))
                    sp.wait_ge(x1_out.sem, x1_out.after(s))
                nat = (x1_dram if cross else x).rearrange("(n p) e -> p n e", p=P)
                apart(sp)
                sp.dma_start(xnat[:, p], nat[:, bass.ds(s * NT, NT), :]).then_inc(xnat_in.sems[p], 16)

            n = 0
            for dst, src in ((cst, consts), (small, tables), (w_qk, wqk_self), (w_v, wv_self)):
                sp.dma_start(dst[:], src).then_inc(cst_in, 16)
                n += 1
            load(0, False, 0)
            for dst, src in ((gb[:, 0], gains), (gb[:, 1], shifts), (w_o[:], wo_self), (wx_q[:], wq_x),
                             (wx_k[:], wk_x), (wx_v[:], wv_x), (wx_o[:], wo_x), (bo[:, 0], bo_self),
                             (bo[:, 1], bo_x), (bqk[:, 0], bq_x), (bqk[:, 1], bk_x), (bv[:], bv_x),
                             (cs[:], rope), (rw[:], router)):
                sp.dma_start(dst, src).then_inc(cst_in, 16)
                n += 1
            assert n == N_CST

            def step(f, f_cross, b, b_cross, fp):
                last = isinstance(f, int) and f == 2 * B - 1
                if f is not None and not last:
                    nxt_cross = f_cross or (isinstance(f, int) and f == B - 1)
                    load(f + 1, nxt_cross, 1 - fp)
                if b is not None:
                    sp.wait_ge(maxT_ready.sem, maxT_ready.after(b))
                    sp.dma_start(qst[ROWS:ROWS + 1, 1 - fp], nmaxT[:]).then_inc(max_in.sem, 16)
                if f is not None:
                    sp.wait_ge(lo_ready.sem, lo_ready.after(f))
                    sp.wait_ge(mid_ready.sem, mid_ready.after(f))
                    if stack_in.begun(f - 2):
                        sp.wait_ge(stack_in.sem, stack_in.after(f - 2))
                    sp.dma_start(part_dram[fp].rearrange("x q (j p) t -> p (x q j) t", p=P),
                                 th[:].rearrange("p x j t -> p (x j) t")).then_inc(parts_out.sem, 16)
                    sp.wait_ge(parts_out.sem, parts_out.after(f))
                    if scoresT_pe.begun(f - 2):
                        sp.wait_ge(scoresT_pe.sem, scoresT_pe.after(f - 2))
                    for s, parts in enumerate(SLOTS):
                        for q, stack in enumerate((qst, kst)):
                            sp.dma_start(stack[s * D:(s + 1) * D, fp],
                                         part_dram[fp, parts[q], q].rearrange("(h d) t -> d h t", d=D)
                                         ).then_inc(stack_in.sem, 16)
                if b is not None:
                    sp.wait_ge(xo_ready.sem, xo_ready.after(b))
                    apart(sp)
                    if b_cross:
                        dst = acc_dram[0:N, :].rearrange("(n p) e -> p n e", p=P)
                        sp.dma_start(dst[:, bass.ds((b - B) * NT, NT), :], pay[:, :, 0:E]
                                     ).then_inc(x2_out.sem, 16)
                    else:
                        dst = x1_dram.rearrange("(n p) e -> p n e", p=P)
                        sp.dma_start(dst[:, bass.ds(b * NT, NT), :], xo[:]).then_inc(x1_out.sem, 16)

            over(step, sp.Fori)
            sp.wait_ge(x1_out.sem, 16 * B)
            sp.wait_ge(x2_out.sem, x2_out.after(2 * B - 1))

            sp.wait_ge(xo_ready.sem, xo_ready.after(2 * B - 1))
            sp.dma_start(b1s, b1).then_inc(biases_in, 16)
            sp.dma_start(b2s, b2).then_inc(biases_in, 16)
            sp.wait_ge(table_ready, 3)
            sp.dma_start(xs_dram[PADS:PADS + P, :], pay[:, 0, :]).then_inc(pads_out, 16)
            sp.dma_start(acc_dram[N:N + P, :], pay[:, 0, 0:E]).then_inc(pads_out, 16)
            sp.wait_ge(pads_out, 32)
            sp.wait_ge(pads_scattered, 16 * NE)

            def tile(f, b, fp):
                if f is None:
                    return
                apart(sp)
                first = sp.value_load(tbli[0:1, 1, bass.ds(f, 1)], min_val=0, max_val=PADS)
                if meta_ready.begun(f - 2):
                    sp.wait_ge(meta_ready.sem, meta_ready.after(f - 2))
                apart(sp)
                if xsT_pe.begun(f - 2):
                    sp.wait_ge(xsT_pe.sem, xsT_pe.after(f - 2))
                apart(sp)
                sp.dma_start(rows[:, fp, :], xs_dram[bass.ds(first, P), :]).then_inc(rows_in.sems[fp], 16)

            over_tiles(tile, sp.Fori)
            sp.wait_ge(added.sem, added.after(TILES - 1))
            acc = acc_dram[0:N, :].rearrange("(g n p) e -> g p n e", p=P, n=LNB)
            res = out.rearrange("(g n p) e -> g p n e", p=P, n=LNB)
            n_groups = N // P // LNB

            def load_ln(g, p):
                sp.dma_start(lnx[:, p], acc[bass.ds(g, 1)].rearrange("o p n e -> (o p) n e")
                             ).then_inc(ln_in.sems[p], 16)

            def store_ln(g, p):
                sp.wait_ge(ln_ready.sem, ln_ready.after(g))
                apart(sp)
                sp.dma_start(res[bass.ds(g, 1)].rearrange("o p n e -> (o p) n e"), lnx[:, p]
                             ).then_inc(ln_out.sem, 16)

            load_ln(0, 0)
            load_ln(1, 1)

            with sp.Fori(0, n_groups // 2 - 1) as i:
                for p in range(2):
                    store_ln(2 * i + p, p)
                    sp.wait_ge(ln_out.sem, ln_out.after(2 * i + p))
                    apart(sp)
                    load_ln(2 * i + 2 + p, p)
            for p in range(2):
                store_ln(n_groups - 2 + p, p)
            sp.wait_ge(ln_out.sem, ln_out.after(n_groups - 1))

        @block.tensor
        def _(pe):
            pe.wait_ge(cst_in, 16 * N_CST)
            pe.wait_ge(cst_ready, N_READY)

            def turn_x1(f, fp):
                pe.wait_ge(xnat_in.sems[fp], xnat_in.after(f, fp))
                if onT_ready.begun(f - 2):
                    pe.wait_ge(onT_ready.sem, onT_ready.after(f - 2))
                if x1T_ready.begun(f - 1):
                    pe.wait_ge(x1T_ready.sem, x1T_ready.after(f - 1))
                for t in range(NT):
                    for c in range(KC):
                        o = (c * NT + t) * P
                        ins = pe.transpose(M0[:, o:o + P], xnat[:, fp, t, c * P:(c + 1) * P], ident[:])
                ins.then_inc(x1T_pe.sem, 1)

            def project_v(f, cross, fp, b):
                if b is not None:
                    pe.wait_ge(maxT_ready.sem, maxT_ready.after(b))
                w = wx_v if cross else w_v
                for t in range(NT):
                    for c in range(KC):
                        ins = pe.matmul(M1[:, t * E:(t + 1) * E], xin[:, fp, c, t * P:(t + 1) * P],
                                        w[:, c, :], start=(c == 0), stop=(c == KC - 1))
                ins.then_inc(v_pe.sem, 1)

            def project_qk(f, cross, fp, t):
                if t:
                    pe.wait_ge(qk_ready.sem, qk_ready.after(f, t))
                else:
                    pe.wait_ge(xin_in.sems[fp], xin_in.after(f, fp))
                    if hi_ready.begun(f - 1):
                        pe.wait_ge(hi_ready.sem, hi_ready.after(f - 1))
                    if rest_ready.begun(f - 1):
                        pe.wait_ge(rest_ready.sem, rest_ready.after(f - 1))
                    if onT_ready.begun(f - 2):
                        pe.wait_ge(onT_ready.sem, onT_ready.after(f - 2))
                if cross:
                    pe.wait_ge(x1T_ready.sem, x1T_ready.after(f))
                    for w, a, o in ((wx_q, x1T[:], 0), (wx_k, xin[:, fp], E)):
                        for c in range(KC):
                            ins = pe.matmul(M0[:, o:o + E], a[:, c, t * P:(t + 1) * P], w[:, c, :],
                                            start=(c == 0), stop=(c == KC - 1))
                else:
                    for c in range(KC):
                        ins = pe.matmul(M0, xin[:, fp, c, t * P:(t + 1) * P], w_qk[:, c, :],
                                        start=(c == 0), stop=(c == KC - 1))
                ins.then_inc(qk_pe.sem, 1)

            def scores(b, cross, bp, u):
                t, g = divmod(u, NG)
                nk = keys_of(cross, t)
                if u == 0:
                    pe.wait_ge(stack_in.sem, stack_in.after(b))
                if u >= 2:
                    pe.wait_ge(max_ready.sem, max_ready.after(b, u - 1))
                else:
                    if exp_ready.begun(b - 1):
                        pe.wait_ge(exp_ready.sem, exp_ready.after(b - 1))
                for i in range(GRP):
                    h = GRP * g + i
                    o = S[u % 2][:, i * nk:(i + 1) * nk]
                    q = qst[0:ROWS, bp, h, t * P:(t + 1) * P]
                    if cross:
                        ins = pe.matmul(o, q, kst[0:ROWS, bp, h, 0:nk], start=True, stop=True)
                        continue
                    if t:
                        pe.matmul(o[:, 0:t * P], q, kst[0:ROWS, bp, h, 0:t * P], start=True, stop=True)
                    pe.matmul(o[:, t * P:nk], q, kst[0:ROWS, bp, h, t * P:nk], start=True, stop=False)
                    ins = pe.matmul(o[:, t * P:nk], identb[:], maskb[:], start=False, stop=True)
                ins.then_inc(scores_pe.sem, 1)

            def turn_max(b):
                pe.wait_ge(max_ready.sem, max_ready.after(b))
                if y_link.begun(b - 1, 1):
                    pe.wait_ge(y_link.sem, y_link.after(b - 1, 1))
                if max_in.begun(b - 1):
                    pe.wait_ge(max_in.sem, max_in.after(b - 1))
                for t in range(NT):
                    ins = pe.transpose(M1[0:H, t * P:(t + 1) * P], nmax[:, t, :], ident[:])
                ins.then_inc(maxT_pe.sem, 1)

            def scores_T(b, cross, bp, u):
                g, kt = divmod(u, NT)
                q0 = queries_of(cross, kt)
                nq = T - q0
                if u == 0:
                    pe.wait_ge(max_in.sem, max_in.after(b))
                if u >= 2:
                    pe.wait_ge(exp_ready.sem, exp_ready.after(b, u - 1))
                for i in range(GRP):
                    h = GRP * g + i
                    ins = pe.matmul(S[u % 2][:, i * nq:(i + 1) * nq],
                                    kst[:, bp, h, kt * P:(kt + 1) * P], qst[:, bp, h, q0:T],
                                    start=True, stop=True)
                ins.then_inc(scoresT_pe.sem, 1)

            def weigh(b, cross, bp, u):
                g, kt = divmod(u, NT)
                q0 = queries_of(cross, kt)
                nq = T - q0
                if u == 0:
                    if oT_a.begun(b - 1):
                        pe.wait_ge(oT_a.sem, oT_a.after(b - 1))
                    if oT_b.begun(b - 1):
                        pe.wait_ge(oT_b.sem, oT_b.after(b - 1))
                if cross:
                    pe.wait_ge(exp_ready.sem, exp_ready.after(b, u + 1))
                else:
                    pe.wait_ge(masked.sem, masked.after(b, u + 1))
                parts = ((0, T),) if cross else ((0, P), (P, T)) if kt == 0 else ((P, T),)
                for lo, hi in parts:
                    whole = not cross and hi == P
                    for i in range(GRP):
                        ins = pe.matmul(O[32 * i:32 * i + 32, g * T + lo:g * T + hi],
                                        vaug[:, bp, kt, GRP * g + i, :], pT[:, u % 3, i, lo - q0:hi - q0],
                                        start=(kt == 0), stop=(kt == NT - 1 or whole))
                ins.then_inc(pv_pe.sem, 1)

            def turn_qk(f, cross, b, has_back, t):
                if cross:
                    pe.wait_ge(rope_link.sem, rope_link.after(f))
                else:
                    pe.wait_ge(gain_link.sem, gain_link.after(f))
                M = (M0, M1)[t]
                if has_back and routes_last(b, cross):
                    if t == 0 and x2T_ready.begun(b - 1):
                        pe.wait_ge(x2T_ready.sem, x2T_ready.after(b - 1))
                    if t == 1 and rank_ready.begun(b - 1):
                        pe.wait_ge(rank_ready.sem, rank_ready.after(b - 1))
                if t == 0:
                    pe.wait_ge(qk_ready.sem, qk_ready.after(f))
                else:
                    pe.wait_ge(v_ready.sem, v_ready.after(f))
                for j in range(4):
                    ins = pe.transpose(M[:, j * P:(j + 1) * P], qkn[:, t, j * P:(j + 1) * P], ident[:])
                ins.then_inc(turned.sem, 1)

            def turn_o(b, f, has_front):
                for t in range(NT):
                    M = (M0, M1)[t]
                    if has_front:
                        pe.wait_ge(rest_ready.sem, rest_ready.after(f, t + 1))
                        pe.wait_ge(hi_ready.sem, hi_ready.after(f, t + 1))
                    elif t == 0:
                        if x2T_ready.begun(b - 1):
                            pe.wait_ge(x2T_ready.sem, x2T_ready.after(b - 1))
                    else:
                        pe.wait_ge(maxT_ready.sem, maxT_ready.after(b))
                        pe.wait_ge(rank_ready.sem, rank_ready.after(b - 1))
                    if t == 0:
                        pe.wait_ge(oT_a.sem, oT_a.after(b))
                        pe.wait_ge(oT_b.sem, oT_b.after(b))
                    for g in range(NG):
                        ins = pe.transpose(M[:, g * P:(g + 1) * P], oT[:, g, t * P:(t + 1) * P], ident[:])
                    ins.then_inc(o_pe.sem, 1)

            def project_o(b, cross):
                pe.wait_ge(on_ready.sem, on_ready.after(b))
                for t in range(NT):
                    for c in range(KC):
                        o = (c * NT + t) * P
                        ins = pe.transpose(M0[:, o:o + P], on[:, t, c * P:(c + 1) * P], ident[:])
                ins.then_inc(onT_pe.sem, 1)
                pe.wait_ge(onT_ready.sem, onT_ready.after(b))
                w = wx_o if cross else w_o
                for t in range(NT):
                    for c in range(KC):
                        ins = pe.matmul(M1[:, t * E:(t + 1) * E], onT[:, c, t * P:(t + 1) * P],
                                        w[:, c, :], start=(c == 0), stop=(c == KC - 1))
                ins.then_inc(wo_pe.sem, 1)

            def turn_x2(b, f):
                pe.wait_ge(xo_ready.sem, xo_ready.after(b))
                if logits_pe.begun(b - 1):
                    pe.wait_ge(logits_pe.sem, logits_pe.after(b - 1))
                if f is not None:
                    pe.wait_ge(qk_ready.sem, qk_ready.after(f))
                pe.wait_ge(onT_ready.sem, onT_ready.after(b))
                for t in range(NT):
                    for c in range(KC):
                        o = (c * NT + t) * P
                        ins = pe.transpose(M0[:, o:o + P], pay[:, t, c * P:(c + 1) * P], ident[:])
                ins.then_inc(x2T_pe.sem, 1)

            def rate(b, f, last_max):
                pe.wait_ge(x2T_ready.sem, x2T_ready.after(b))
                if f is not None:
                    pe.wait_ge(v_ready.sem, v_ready.after(f))
                if last_max:
                    pe.wait_ge(maxT_ready.sem, maxT_ready.after(b + 1))
                pe.wait_ge(y_link.sem, y_link.after(b, 1))
                for t in range(NT):
                    for c in range(KC):
                        ins = pe.matmul(M1[:, t * NE:(t + 1) * NE], x2T[:, c, t * P:(t + 1) * P],
                                        rw[:, c, :], start=(c == 0), stop=(c == KC - 1))
                ins.then_inc(logits_pe.sem, 1)

            def count_tokens(b):
                pe.wait_ge(hot_ready.sem, hot_ready.after(b))
                o = 2 * NE
                pe.matmul(M1[:, o:o + NE], trib[:], ohb[:, 0, :], start=True, stop=True)
                pe.matmul(M1[:, o + NE:o + 2 * NE], onesb[:], ohb[:, 0, :], start=True, stop=False)
                pe.matmul(M1[:, o + NE:o + 2 * NE], trib[:], ohb[:, 1, :], start=False, stop=True)
                pe.matmul(M1[:, o + 2 * NE:o + 3 * NE], onesb[:], ohb[:, 0, :], start=True, stop=False)
                pe.matmul(M1[:, o + 2 * NE:o + 3 * NE], onesb[:], ohb[:, 1, :], start=False, stop=True
                          ).then_inc(rank_pe.sem, 1)

            def step(f, f_cross, b, b_cross, fp):
                front, back = f is not None, b is not None
                bp = 1 - fp
                if front:
                    if f_cross:
                        turn_x1(f, fp)
                    project_qk(f, f_cross, fp, 0)
                if back:
                    for u in range(NU // 2):
                        scores(b, b_cross, bp, u)
                if front:
                    project_qk(f, f_cross, fp, 1)
                if back:
                    for u in range(NU // 2, NU):
                        scores(b, b_cross, bp, u)
                    turn_max(b)
                if front:
                    project_v(f, f_cross, fp, b)
                if back:
                    scores_T(b, b_cross, bp, 0)
                    for u in range(1, NU):
                        scores_T(b, b_cross, bp, u)
                        weigh(b, b_cross, bp, u - 1)
                        if routes_last(b, b_cross):
                            if u == 1:
                                turn_x2(b - 1, f)
                            elif u == 2:
                                rate(b - 1, f, True)
                            elif u == TURN_AT:
                                count_tokens(b - 1)
                        if front and u == TURN_AT:
                            turn_qk(f, f_cross, b, back, 0)
                            turn_qk(f, f_cross, b, back, 1)
                elif front:
                    turn_qk(f, f_cross, b, back, 0)
                    turn_qk(f, f_cross, b, back, 1)
                if back:
                    weigh(b, b_cross, bp, NU - 1)
                    turn_o(b, f, front)
                    project_o(b, b_cross)
                if not front:
                    turn_x2(b, None)
                    rate(b, None, False)
                    count_tokens(b)

            over(step, pe.Fori)
            pe.wait_ge(table_ready, 3)
            pe.wait_ge(moe_in, 32)

            def bank(n, p):
                return PS[:, (2 * n + p) * 512:(2 * n + p + 1) * 512]

            def tile(f, b, fp):
                bp = 1 - fp
                if f is not None:
                    pe.wait_ge(rows_in.sems[fp], rows_in.after(f, fp))
                    if xsT_ready.begun(f - 2):
                        pe.wait_ge(xsT_ready.sem, xsT_ready.after(f - 2))
                    for c in range(KC):
                        ins = pe.transpose(bank(0, fp)[:, c * P:(c + 1) * P], rows[:, fp, c * P:(c + 1) * P],
                                           ident[:])
                    ins.then_inc(xsT_pe.sem, 1)
                if b is not None:
                    pe.wait_ge(hact_ready.sem, hact_ready.after(b))
                    if hT_ready.begun(b - 2):
                        pe.wait_ge(hT_ready.sem, hT_ready.after(b - 2))
                    for c in range(FC):
                        ins = pe.transpose(bank(2, bp)[:, c * P:(c + 1) * P], hact[:, bp, c * P:(c + 1) * P],
                                           ident[:])
                    ins.then_inc(hT_pe.sem, 1)
                if f is not None:
                    e = expert_of(pe, f)
                    pe.wait_ge(xsT_ready.sem, xsT_ready.after(f))
                    if hpre_ready.begun(f - 2):
                        pe.wait_ge(hpre_ready.sem, hpre_ready.after(f - 2))
                    for c in range(KC):
                        w = w1s[:, c, bass.ds(e, 1), :].rearrange("p o f -> p (o f)")
                        ins = pe.matmul(bank(1, fp), xsT[:, fp, c * P:(c + 1) * P], w,
                                        start=(c == 0), stop=(c == KC - 1))
                    ins.then_inc(h_pe.sem, 1)
                if b is not None:
                    e = expert_of(pe, b)
                    pe.wait_ge(hT_ready.sem, hT_ready.after(b))
                    if ye_link.begun(b - 2):
                        pe.wait_ge(ye_link.sem, ye_link.after(b - 2))
                    for c in range(FC):
                        w = w2s[:, c, bass.ds(e, 1), :].rearrange("p o f -> p (o f)")
                        ins = pe.matmul(bank(3, bp)[:, 0:E], hT[:, bp, c * P:(c + 1) * P], w,
                                        start=(c == 0), stop=(c == FC - 1))
                    ins.then_inc(y_pe.sem, 1)

            over_tiles(tile, pe.Fori)

        @block.scalar
        def _(act):
            act.wait_ge(cst_ready, N_READY)

            def copy_x2T(b):
                act.wait_ge(x2T_pe.sem, x2T_pe.after(b))
                act.activation(x2T[:].rearrange("p c t -> p (c t)"), M0, ACT.Copy
                               ).then_inc(x2T_ready.sem, 1)

            def exp_gap(b):
                act.wait_ge(gap_ready.sem, gap_ready.after(b))
                act.activation(pe1[:, 1, :], pe1[:, 0, :], ACT.Exp).then_inc(e_ready.sem, 1)

            def step(f, f_cross, b, b_cross, fp):
                front, back = f is not None, b is not None
                bp = 1 - fp
                if front and f_cross:
                    act.wait_ge(x1T_pe.sem, x1T_pe.after(f))
                    if qk_pe.begun(f - 1):
                        act.wait_ge(qk_pe.sem, qk_pe.after(f - 1))
                    act.activation(x1T[:].rearrange("p c t -> p (c t)"), M0, ACT.Copy
                                   ).then_inc(x1T_ready.sem, 1)
                if front and not f_cross:
                    if turned.begun(f - 1):
                        act.wait_ge(turned.sem, turned.after(f - 1))
                    for t in range(NT):
                        act.wait_ge(qk_pe.sem, qk_pe.after(f, t + 1))
                        act.activation(qkn[:, t, :], M0, ACT.Copy).then_inc(qk_ready.sem, 1)
                if back:
                    act.wait_ge(maxT_pe.sem, maxT_pe.after(b))
                    act.activation(nmaxT[:], M1[0:H, 0:T], ACT.Copy).then_inc(maxT_ready.sem, 1)

                def weights(u):
                    kt = u % NT
                    nq = T - queries_of(b_cross, kt)
                    act.wait_ge(scoresT_pe.sem, scoresT_pe.after(b, u + 1))
                    if u >= 3:
                        act.wait_ge(pv_pe.sem, pv_pe.after(b, u - 2))
                    else:
                        if pv_pe.begun(b - 1):
                            act.wait_ge(pv_pe.sem, pv_pe.after(b - 1))
                    act.activation(pT[:, u % 3, :, 0:nq],
                                   S[u % 2][:, 0:GRP * nq].rearrange("p (h q) -> p h q", h=GRP),
                                   ACT.Exp).then_inc(exp_ready.sem, 1)

                if back:
                    weights(0)
                if front and not f_cross:
                    act.wait_ge(v_pe.sem, v_pe.after(f))
                    if pv_pe.begun(f - 2):
                        act.wait_ge(pv_pe.sem, pv_pe.after(f - 2))
                    act.activation(vaug[:, fp, :, :, 0:D], M1.rearrange("p (t h d) -> p t h d", t=NT, d=D),
                                   ACT.Copy).then_inc(v_ready.sem, 1)
                if back:
                    weights(1)
                if front and not f_cross:
                    act.wait_ge(centered.sem, centered.after(f))
                    act.activation(sq[:], xc[:], ACT.Square).then_inc(squared.sem, 1)
                if back:
                    if routes_last(b, b_cross):
                        copy_x2T(b - 1)
                    for u in range(2, TURN_AT):
                        weights(u)
                    if routes_last(b, b_cross):
                        exp_gap(b - 1)
                if front:
                    if parts_out.begun(f - 1):
                        act.wait_ge(parts_out.sem, parts_out.after(f - 1))
                    for t in range(NT):
                        act.wait_ge(turned.sem, turned.after(f, t + 1))
                        act.activation(th[:, 0, :, t * P:(t + 1) * P],
                                       (M0, M1)[t].rearrange("p (j q) -> p j q", j=4), ACT.Copy
                                       ).then_inc(hi_ready.sem, 1)
                if back:
                    for u in range(TURN_AT, NU):
                        weights(u)
                if back:
                    act.wait_ge(pv_pe.sem, pv_pe.after(b))
                    if o_pe.begun(b - 1):
                        act.wait_ge(o_pe.sem, o_pe.after(b - 1))
                    act.activation(oT[:, 2:4, :], O[:, 512:1024].rearrange("p (g t) -> p g t", g=2),
                                   ACT.Copy).then_inc(oT_b.sem, 1)
                    act.wait_ge(onT_pe.sem, onT_pe.after(b))
                    if wo_pe.begun(b - 1):
                        act.wait_ge(wo_pe.sem, wo_pe.after(b - 1))
                    act.activation(onT[:].rearrange("p c t -> p (c t)"), M0, ACT.Copy
                                   ).then_inc(onT_ready.sem, 1)
                    if not front:
                        copy_x2T(b)
                        exp_gap(b)

            over(step, act.Fori)
            act.wait_ge(table_ready, 3)

            def tile(f, b, fp):
                if f is None:
                    return
                act.wait_ge(xsT_pe.sem, xsT_pe.after(f))
                if h_pe.begun(f - 2):
                    act.wait_ge(h_pe.sem, h_pe.after(f - 2))
                act.activation(xsT[:, fp], PS[:, fp * 512:fp * 512 + E], ACT.Copy
                               ).then_inc(xsT_ready.sem, 1)
                act.wait_ge(hpre_ready.sem, hpre_ready.after(f))
                if hT_pe.begun(f - 2):
                    act.wait_ge(hT_pe.sem, hT_pe.after(f - 2))
                act.activation(hact[:, fp], hpre[:, fp], ACT.Gelu).then_inc(hact_ready.sem, 1)

            over_tiles(tile, act.Fori)

        @block.vector
        def _(dve):
            dve.wait_ge(cst_in, 16 * N_CST)
            dve.tensor_copy(ident[:], cst[:, 0, :]).then_inc(cst_ready, 1)
            dve.tensor_copy(identb[:], cst[:, 0, :]).then_inc(cst_ready, 1)
            dve.tensor_copy(maskb[:], cst[:, 1, :]).then_inc(cst_ready, 1)
            dve.tensor_copy(trib[:], cst[:, 2, :]).then_inc(cst_ready, 1)
            dve.memset(onesb[:], 1.0).then_inc(cst_ready, 1)
            dve.memset(mix[:, 0:2048], 1.0).then_inc(cst_ready, 1)
            dve.memset(kst[ROWS:ROWS + 1], 1.0).then_inc(cst_ready, 1)
            dve.memset(pay[:], 0.0).then_inc(cst_ready, 1)
            dve.tensor_scalar(gb[:].rearrange("p a t q d -> p (a t q d)"),
                              gb[:].rearrange("p a t q d -> p (a t q d)"),
                              float(E) ** -0.25, None, ALU.mult).then_inc(cst_ready, 1)
            dve.tensor_copy(carry[:], iota8_region).then_inc(cst_ready, 1)
            for t in range(NT):
                dve.tensor_scalar(idf[:, t:t + 1], pcol, float(t * P - T), None, ALU.add
                                  ).then_inc(cst_ready, 1)
            dve.wait_ge(cst_ready, N_READY)

            def copy_v(f, fp):
                dve.wait_ge(v_pe.sem, v_pe.after(f))
                if pv_pe.begun(f - 2):
                    dve.wait_ge(pv_pe.sem, pv_pe.after(f - 2))
                src = M1.rearrange("p (t h d) -> p t h d", t=NT, d=D)
                bias = bv[:].rearrange("p (h d) -> p h d", d=D)
                for t in range(NT):
                    ins = dve.tensor_tensor(vaug[:, fp, t, :, 0:D], src[:, t], bias, ALU.add)
                ins.then_inc(v_ready.sem, 1)

            def copy_qk(f, t):
                dve.wait_ge(qk_pe.sem, qk_pe.after(f, t + 1))
                if turned.begun(f - 1):
                    dve.wait_ge(turned.sem, turned.after(f - 1))
                dve.tensor_tensor(qkn[:, t, :], M0, bqk[:].rearrange("p q e -> p (q e)"), ALU.add
                                  ).then_inc(qk_ready.sem, 1)

            def maxima(b, cross, u):
                t, g = divmod(u, NG)
                nk = keys_of(cross, t)
                dve.wait_ge(scores_pe.sem, scores_pe.after(b, u + 1))
                if u == 0:
                    if maxT_pe.begun(b - 1):
                        dve.wait_ge(maxT_pe.sem, maxT_pe.after(b - 1))
                dve.tensor_reduce(nmax[:, t, g * GRP:(g + 1) * GRP],
                                  S[u % 2][:, 0:GRP * nk].rearrange("p (h k) -> p h k", h=GRP),
                                  AX.X, ALU.max, negate=True).then_inc(max_ready.sem, 1)

            def head_norms(f):
                count = norm_link.counter(f)
                dve.wait_ge(qk_ready.sem, qk_ready.after(f))
                gs, hv, v, yy, t0, t1 = (st[:, i, :] for i in range(6))
                dve.tensor_reduce(gs, groups16(qkn), AX.X, ALU.add).then_inc(norm_link.sem, 1)
                dve.wait_ge(norm_link.sem, count())
                if squared.begun(f - 1):
                    dve.wait_ge(squared.sem, squared.after(f - 1))
                dve.scalar_tensor_tensor(out=groups16(xc), in0=bc(gs, D), scalar=-1.0 / D,
                                         in1=groups16(qkn), op0=ALU.mult, op1=ALU.add
                                         ).then_inc(centered.sem, 1)
                dve.wait_ge(squared.sem, squared.after(f))
                dve.tensor_reduce(gs, groups16(sq), AX.X, ALU.add).then_inc(norm_link.sem, 1)
                dve.wait_ge(norm_link.sem, count())
                dve.tensor_scalar(hv, gs, 0.5 / D, 0.5 * EPS, ALU.mult, ALU.add).then_inc(norm_link.sem, 1)
                dve.wait_ge(norm_link.sem, count())
                dve.tensor_scalar(v, gs, 1.0 / D, EPS, ALU.mult, ALU.add).then_inc(norm_link.sem, 1)
                dve.wait_ge(norm_link.sem, count())
                rsqrt_steps(dve, norm_link.sem, count, v, hv, yy, t0, t1)
                dve.tensor_tensor(groups16(qkn), groups16(xc), bc(yy, D), ALU.mult).then_inc(norm_link.sem, 1)
                dve.wait_ge(norm_link.sem, count())

            def rotate(f):
                count = rope_link.counter(f)
                dve.wait_ge(qk_ready.sem, qk_ready.after(f))
                x4, s4 = heads4(qkn), heads4(sq)
                h = D // 2
                dve.tensor_tensor(s4[:, :, :, 0:h], x4[:, :, :, h:D], per_head(cs[:, 1, :, :, 0:h]),
                                  ALU.mult).then_inc(rope_link.sem, 1)
                dve.wait_ge(rope_link.sem, count())
                dve.tensor_tensor(s4[:, :, :, h:D], x4[:, :, :, 0:h], per_head(cs[:, 1, :, :, h:D]),
                                  ALU.mult).then_inc(rope_link.sem, 1)
                dve.wait_ge(rope_link.sem, count())
                dve.wait_ge(cosined.sem, cosined.after(f))
                dve.tensor_tensor(qkn[:], xc[:], sq[:], ALU.add).then_inc(rope_link.sem, 1)
                dve.wait_ge(rope_link.sem, count())

            def finish(b, cross, bp):
                count = y_link.counter(b)
                dve.wait_ge(wo_pe.sem, wo_pe.after(b))
                dve.wait_ge(xb_ready.sem, xb_ready.after(b))
                dve.tensor_tensor(y[:], M1.rearrange("p (t e) -> p t e", t=NT), xb[:, bp], ALU.add
                                  ).then_inc(y_link.sem, 1)
                dve.wait_ge(y_link.sem, count())
                for t in range(NT):
                    dve.bn_stats(bst[:, t, :], y[:, t, :]).then_inc(y_link.sem, 1)
                    dve.wait_ge(y_link.sem, count())
                for t in range(NT):
                    apart(dve)
                    dve.bn_aggr(mv[:, t, :], bst[:, t, :]).then_inc(y_link.sem, 1)
                    dve.wait_ge(y_link.sem, count())
                v, hv, yy, t0, t1 = (ls[:, i, 0:NT] for i in range(5))
                dve.tensor_scalar(v, mv[:, 0:NT, 1], EPS, None, ALU.add).then_inc(y_link.sem, 1)
                dve.wait_ge(y_link.sem, count())
                dve.tensor_scalar(hv, mv[:, 0:NT, 1], 0.5, 0.5 * EPS, ALU.mult, ALU.add).then_inc(y_link.sem, 1)
                dve.wait_ge(y_link.sem, count())
                rsqrt_steps(dve, y_link.sem, count, v, hv, yy, t0, t1)
                if cross:
                    if x2_out.begun(b - 1):
                        dve.wait_ge(x2_out.sem, x2_out.after(b - 1))
                    if scattered.begun(b - 1):
                        dve.wait_ge(scattered.sem, scattered.after(b - 1))
                    if x2T_pe.begun(b - 1):
                        dve.wait_ge(x2T_pe.sem, x2T_pe.after(b - 1))
                else:
                    if x1_out.begun(b - 1):
                        dve.wait_ge(x1_out.sem, x1_out.after(b - 1))
                for t in range(NT):
                    dst = pay[:, t, 0:E] if cross else xo[:, t, :]
                    dve.tensor_scalar(dst, y[:, t, :], mv[:, t, 0:1], ls[:, 2, t:t + 1],
                                      ALU.subtract, ALU.mult).then_inc(xo_ready.sem, 1)

            def choose(b):
                count = router_link.counter(b)
                dve.wait_ge(logits_pe.sem, logits_pe.after(b))
                dve.tensor_copy(lg[:], M1[:, 0:2 * NE].rearrange("p (t e) -> p t e", t=NT)
                                ).then_inc(router_link.sem, 1)
                dve.wait_ge(router_link.sem, count())
                for t in range(NT):
                    apart(dve)
                    dve.max(mx8[:, t, :], lg[:, t, :]).then_inc(router_link.sem, 1)
                    dve.wait_ge(router_link.sem, count())
                for t in range(NT):
                    apart(dve)
                    dve.max_index(ix8[:, t, :], mx8[:, t, :], lg[:, t, :]).then_inc(router_link.sem, 1)
                    dve.wait_ge(router_link.sem, count())
                dve.tensor_tensor(pe1[:, 0, :], mx8[:, :, 1], mx8[:, :, 0], ALU.subtract
                                  ).then_inc(gap_ready.sem, 1)
                dve.tensor_copy(ixf[:], ix8[:, :, 0:TOPK]).then_inc(router_link.sem, 1)
                dve.wait_ge(router_link.sem, count())
                i4 = iota8.unsqueeze(1).to_broadcast([P, NT * TOPK, NE])
                dve.tensor_tensor(oh[:].rearrange("p t k e -> p (t k) e"), i4,
                                  bc(ixf[:].rearrange("p t k -> p (t k)"), NE), ALU.is_equal
                                  ).then_inc(router_link.sem, 1)
                dve.wait_ge(router_link.sem, count())
                dve.tensor_tensor(ohb[:], oh[:, :, 0, :], oh[:, :, 1, :], ALU.add
                                  ).then_inc(hot_ready.sem, 1)
                dve.wait_ge(e_ready.sem, e_ready.after(b))
                dve.tensor_scalar(pe1[:, 2, :], pe1[:, 1, :], 1.0, None, ALU.add).then_inc(router_link.sem, 1)
                dve.wait_ge(router_link.sem, count())
                dve.reciprocal(prob[:, :, 0], pe1[:, 2, :]).then_inc(router_link.sem, 1)
                dve.wait_ge(router_link.sem, count())
                dve.tensor_tensor(prob[:, :, 1], prob[:, :, 0], pe1[:, 1, :], ALU.mult
                                  ).then_inc(router_link.sem, 1)
                dve.wait_ge(router_link.sem, count())
                dve.tensor_tensor(sel[:].rearrange("p t k e -> p (t k) e"),
                                  oh[:].rearrange("p t k e -> p (t k) e"),
                                  bc(prob[:].rearrange("p t k -> p (t k)"), NE), ALU.mult
                                  ).then_inc(router_link.sem, 1)
                dve.wait_ge(router_link.sem, count())
                dve.tensor_tensor(pay[:, :, COL_CW:COL_CW + NE], sel[:, :, 0, :], sel[:, :, 1, :],
                                  ALU.add).then_inc(router_link.sem, 1)
                dve.wait_ge(router_link.sem, count())
                dve.tensor_scalar(idf[:], idf[:], float(T), None, ALU.add).then_inc(router_link.sem, 1)
                dve.wait_ge(router_link.sem, count())
                dve.tensor_copy(pay[:, :, COL_ID], idf[:]).then_inc(router_link.sem, 1)
                dve.wait_ge(router_link.sem, count())
                dve.wait_ge(rank_pe.sem, rank_pe.after(b))
                c2 = carry[:].unsqueeze(1).to_broadcast([P, NT, NE])
                dve.tensor_tensor(rank[:], M1[:, 2 * NE:4 * NE].rearrange("p (t e) -> p t e", t=NT),
                                  c2, ALU.add).then_inc(router_link.sem, 1)
                dve.wait_ge(router_link.sem, count())
                dve.tensor_tensor(carry[:], M1[:, 4 * NE:5 * NE], carry[:], ALU.add
                                  ).then_inc(rank_ready.sem, 1)
                for t in range(NT):
                    r2 = rank[:, t, :].unsqueeze(1).to_broadcast([P, TOPK, NE])
                    dve.tensor_tensor(sel[:, t], oh[:, t], r2, ALU.mult).then_inc(router_link.sem, 1)
                    dve.wait_ge(router_link.sem, count())
                dve.tensor_reduce(posf[:], sel[:].rearrange("p t k e -> p (t k) e"), AX.X, ALU.add
                                  ).then_inc(router_link.sem, 1)
                dve.wait_ge(router_link.sem, count())
                dve.tensor_copy(posi[:], posf[:]).then_inc(row_ready.sem, 1)

            def step(f, f_cross, b, b_cross, fp):
                front, back = f is not None, b is not None
                bp = 1 - fp
                if front and f_cross:
                    copy_qk(f, 0)
                if back:
                    for u in range(NU // 2):
                        maxima(b, b_cross, u)
                if front and f_cross:
                    copy_qk(f, 1)
                if back:
                    for u in range(NU // 2, NU):
                        maxima(b, b_cross, u)
                if front:
                    if f_cross:
                        copy_v(f, fp)
                        rotate(f)
                    else:
                        head_norms(f)
                        count = gain_link.counter(f)
                        for a in range(2):
                            dve.tensor_tensor(heads4(qkn), heads4(qkn), per_head(gb[:, a]), (ALU.mult, ALU.add)[a]
                                              ).then_inc(gain_link.sem, 1)
                            dve.wait_ge(gain_link.sem, count())
                if back and routes_last(b, b_cross):
                    choose(b - 1)
                if front:
                    for t in range(NT):
                        dve.wait_ge(turned.sem, turned.after(f, t + 1))
                        dve.wait_ge(hi_ready.sem, hi_ready.after(f, t + 1))
                        if lo_ready.begun(f - 1, t + 1):
                            dve.wait_ge(lo_ready.sem, lo_ready.after(f - 1, t + 1))
                        dve.tensor_tensor(rr[:, t], (M0, M1)[t].rearrange("p (j q) -> p j q", j=4),
                                          th[:, 0, :, t * P:(t + 1) * P], ALU.subtract
                                          ).then_inc(rest_ready.sem, 1)
                        dve.wait_ge(rest_ready.sem, rest_ready.after(f, t + 1))
                        dve.tensor_copy(th[:, 1, :, t * P:(t + 1) * P], rr[:, t]).then_inc(mid_ready.sem, 1)
                        dve.wait_ge(mid_ready.sem, mid_ready.after(f, t + 1))
                        dve.tensor_tensor(th[:, 2, :, t * P:(t + 1) * P], rr[:, t],
                                          th[:, 1, :, t * P:(t + 1) * P], ALU.subtract
                                          ).then_inc(lo_ready.sem, 1)
                if back:
                    dve.wait_ge(pv_pe.sem, pv_pe.after(b))
                    if o_pe.begun(b - 1):
                        dve.wait_ge(o_pe.sem, o_pe.after(b - 1))
                    dve.tensor_copy(oT[:, 0:2, :], O[:, 0:512].rearrange("p (g t) -> p g t", g=2)
                                    ).then_inc(oT_a.sem, 1)
                    for t in range(NT):
                        dve.wait_ge(o_pe.sem, o_pe.after(b, t + 1))
                        m = (M0, M1)[t].rearrange("p (h d) -> p h d", d=32)
                        dve.reciprocal(rec[:, t, :], m[:, :, D]).then_inc(rec_ready.sem, 1)
                        dve.wait_ge(rec_ready.sem, rec_ready.after(b, t + 1))
                        if onT_pe.begun(b - 1):
                            dve.wait_ge(onT_pe.sem, onT_pe.after(b - 1))
                        dve.tensor_tensor(on[:, t, :].rearrange("p (h d) -> p h d", d=D), m[:, :, 0:D],
                                          bc(rec[:, t, :], D), ALU.mult).then_inc(on_ready.sem, 1)
                    finish(b, b_cross, bp)
                    if not front:
                        choose(b)

            over(step, dve.Fori)

            count = table_link.counter(0)
            dve.wait_ge(scattered.sem, scattered.after(2 * B - 1))
            dve.wait_ge(x2_out.sem, x2_out.after(2 * B - 1))
            dve.wait_ge(x2T_pe.sem, x2T_pe.after(2 * B - 1))
            dve.wait_ge(rank_ready.sem, rank_ready.after(2 * B - 1))
            dve.memset(pay[:, 0, :], 0.0).then_inc(table_link.sem, 1)
            dve.wait_ge(table_link.sem, count())
            dve.tensor_copy(pay[:, 0, COL_ID:COL_ID + 1], idcol).then_inc(table_ready, 1)
            dve.tensor_scalar(cnt[:, 0], carry[:], pcol, None, ALU.add).then_inc(table_link.sem, 1)
            dve.wait_ge(table_link.sem, count())
            dve.tensor_copy(cnti[:, 0], cnt[:, 0]).then_inc(table_ready, 1)
            dve.tensor_tensor(cnt[:, 1], carry[:], iota8_region, ALU.subtract).then_inc(table_link.sem, 1)
            dve.wait_ge(table_link.sem, count())
            dve.tensor_scalar(cnti[:, 1], cnt[:, 1], float(P - 1), None, ALU.add).then_inc(table_link.sem, 1)
            dve.wait_ge(table_link.sem, count())
            dve.tensor_scalar(cnti[:, 1], cnti[:, 1], 7, None, ALU.logical_shift_right
                              ).then_inc(table_link.sem, 1)
            dve.wait_ge(table_link.sem, count())
            dve.tensor_copy(cnt[:, 2], cnti[:, 1]).then_inc(table_link.sem, 1)
            dve.wait_ge(table_link.sem, count())
            w88 = sq[:].rearrange("p t e -> p (t e)")[:, 0:NE * NE].rearrange("p (a b) -> p a b", a=NE)
            dve.tensor_tensor(w88, tri8, cnt[:, 2].unsqueeze(1).to_broadcast([P, NE, NE]), ALU.mult
                              ).then_inc(table_link.sem, 1)
            dve.wait_ge(table_link.sem, count())
            dve.tensor_reduce(cnt[:, 3], w88, AX.X, ALU.add).then_inc(table_link.sem, 1)
            dve.wait_ge(table_link.sem, count())
            dve.tensor_tensor(cnt[:, 4], cnt[:, 3], cnt[:, 2], ALU.subtract).then_inc(table_link.sem, 1)
            dve.wait_ge(table_link.sem, count())
            dve.scalar_tensor_tensor(out=cnt[:, 5], in0=cnt[:, 4], scalar=-float(P), in1=iota8_region,
                                     op0=ALU.mult, op1=ALU.add).then_inc(table_link.sem, 1)
            dve.wait_ge(table_link.sem, count())
            wj = [a[:].rearrange("p t e -> p (t e)")[:, 0:TILES * NE].rearrange("p (j e) -> p j e", e=NE)
                  for a in (sq, xc)]

            def every_j(ap):
                return ap.unsqueeze(1).to_broadcast([P, TILES, NE])

            dve.tensor_tensor(wj[0], every_j(cnt[:, 3]), bc(jrow, NE), ALU.is_le).then_inc(table_link.sem, 1)
            dve.wait_ge(table_link.sem, count())
            dve.tensor_reduce(tbl[:, 0], wj[0], AX.X, ALU.add).then_inc(table_link.sem, 1)
            dve.wait_ge(table_link.sem, count())
            dve.tensor_tensor(wj[0], every_j(iota8), bc(tbl[:, 0], NE), ALU.is_equal
                              ).then_inc(table_link.sem, 1)
            dve.wait_ge(table_link.sem, count())
            dve.tensor_scalar(tbl[:, 1], jrow, float(P), None, ALU.mult).then_inc(table_link.sem, 1)
            dve.wait_ge(table_link.sem, count())
            dve.tensor_tensor(wj[1], every_j(cnt[:, 5]), bc(tbl[:, 1], NE), ALU.add).then_inc(table_link.sem, 1)
            dve.wait_ge(table_link.sem, count())
            dve.tensor_tensor(wj[1], wj[1], wj[0], ALU.mult).then_inc(table_link.sem, 1)
            dve.wait_ge(table_link.sem, count())
            dve.tensor_reduce(tbl[:, 1], wj[1], AX.X, ALU.add).then_inc(table_link.sem, 1)
            dve.wait_ge(table_link.sem, count())
            t9 = sq[:, 0, 0:TILES]
            dve.tensor_scalar(t9, tbl[:, 0], float(NE), float(PADS), ALU.is_equal, ALU.mult
                              ).then_inc(table_link.sem, 1)
            dve.wait_ge(table_link.sem, count())
            dve.tensor_tensor(tbl[:, 1], tbl[:, 1], t9, ALU.add).then_inc(table_link.sem, 1)
            dve.wait_ge(table_link.sem, count())
            dve.tensor_scalar(tbl[:, 0], tbl[:, 0], float(NE - 1), None, ALU.min).then_inc(table_link.sem, 1)
            dve.wait_ge(table_link.sem, count())
            dve.tensor_copy(tbli[:], tbl[:]).then_inc(table_ready, 1)
            dve.wait_ge(table_ready, 3)
            dve.wait_ge(biases_in, 32)

            def tile(f, b, fp):
                bp = 1 - fp
                if f is not None:
                    dve.wait_ge(rows_in.sems[fp], rows_in.after(f, fp))
                    dve.tensor_copy(meta[:, fp], rows[:, fp, COL_CW:COL_ID + 1]).then_inc(meta_ready.sem, 1)
                if b is not None:
                    dve.wait_ge(hT_pe.sem, hT_pe.after(b))
                    if y_pe.begun(b - 2):
                        dve.wait_ge(y_pe.sem, y_pe.after(b - 2))
                    dve.tensor_copy(hT[:, bp], PS[:, (4 + bp) * 512:(5 + bp) * 512]
                                    ).then_inc(hT_ready.sem, 1)
                if f is not None:
                    e = expert_of(dve, f)
                    dve.wait_ge(h_pe.sem, h_pe.after(f))
                    if hact_ready.begun(f - 2):
                        dve.wait_ge(hact_ready.sem, hact_ready.after(f - 2))
                    dve.tensor_tensor(hpre[:, fp], PS[:, (2 + fp) * 512:(3 + fp) * 512],
                                      b1s[:, bass.ds(e, 1), :].rearrange("p o f -> p (o f)"), ALU.add
                                      ).then_inc(hpre_ready.sem, 1)
                if b is not None:
                    e = expert_of(dve, b)
                    count = ye_link.counter(b)
                    dve.wait_ge(y_pe.sem, y_pe.after(b))
                    if added.begun(b - 2):
                        dve.wait_ge(added.sem, added.after(b - 2))
                    dve.tensor_tensor(ye[:, bp], PS[:, (6 + bp) * 512:(6 + bp) * 512 + E],
                                      b2s[:, bass.ds(e, 1), :].rearrange("p o f -> p (o f)"), ALU.add
                                      ).then_inc(ye_link.sem, 1)
                    dve.wait_ge(ye_link.sem, count())
                    dve.tensor_scalar(ye[:, bp], ye[:, bp], meta[:, bp, bass.ds(e, 1)], None,
                                      ALU.mult).then_inc(ye_link.sem, 1)
                    dve.wait_ge(ye_link.sem, count())
                    dve.tensor_copy(rowid[:, bp], meta[:, bp, NE:NE + 1]).then_inc(ye_link.sem, 1)
                    dve.wait_ge(ye_link.sem, count())

            over_tiles(tile, dve.Fori)

            def norm(g, p):
                count = ln_link.counter(g)
                dve.wait_ge(ln_in.sems[p], ln_in.after(g, p))
                for n in range(LNB):
                    dve.bn_stats(bst[:, n, :], lnx[:, p, n, :]).then_inc(ln_link.sem, 1)
                    dve.wait_ge(ln_link.sem, count())
                for n in range(LNB):
                    apart(dve)
                    dve.bn_aggr(mv[:, n, :], bst[:, n, :]).then_inc(ln_link.sem, 1)
                    dve.wait_ge(ln_link.sem, count())
                v, hv, yy, t0, t1 = (ls[:, i, :] for i in range(5))
                dve.tensor_scalar(v, mv[:, :, 1], EPS, None, ALU.add).then_inc(ln_link.sem, 1)
                dve.wait_ge(ln_link.sem, count())
                dve.tensor_scalar(hv, mv[:, :, 1], 0.5, 0.5 * EPS, ALU.mult, ALU.add).then_inc(ln_link.sem, 1)
                dve.wait_ge(ln_link.sem, count())
                rsqrt_steps(dve, ln_link.sem, count, v, hv, yy, t0, t1)
                for n in range(LNB):
                    ins = dve.tensor_scalar(lnx[:, p, n, :], lnx[:, p, n, :], mv[:, n, 0:1],
                                            ls[:, 2, n:n + 1], ALU.subtract, ALU.mult)
                    ins.then_inc(ln_ready.sem, 1)
                dve.wait_ge(ln_ready.sem, ln_ready.after(g))

            over_ln(norm, dve.Fori)

        @block.gpsimd
        def _(pool):
            pool.wait_ge(cst_in, 16 * N_CST)
            pool.dma_start(w1s[:], w1).then_inc(moe_in, 16)
            pool.dma_start(w2s[:], w2).then_inc(moe_in, 16)
            pool.wait_ge(cst_ready, N_READY)

            def scatter(b):
                pool.wait_ge(row_ready.sem, row_ready.after(b))
                pool.wait_ge(router_link.sem, router_link.after(b))
                apart(pool)
                for t in range(NT):
                    for k in range(TOPK):
                        c = t * TOPK + k
                        pool.indirect_dma_start(
                            out=xs_dram, out_offset=bass.IndirectOffsetOnAxis(ap=posi[:, c:c + 1], axis=0),
                            in_=pay[:, t, :], in_offset=None).then_inc(scattered.sem, 16)

            def step(f, f_cross, b, b_cross, fp):
                front, back = f is not None, b is not None
                if front:
                    pool.wait_ge(xnat_in.sems[fp], xnat_in.after(f, fp))
                    if y_link.begun(f - 2):
                        pool.wait_ge(y_link.sem, y_link.after(f - 2))
                    for t in range(NT):
                        ins = pool.tensor_tensor(xb[:, fp, t, :], xnat[:, fp, t, :],
                                                 bo[:, int(f_cross), :], ALU.add)
                    ins.then_inc(xb_ready.sem, 1)
                if front and f_cross:
                    pool.wait_ge(qk_ready.sem, qk_ready.after(f))
                    if rope_link.begun(f - 1):
                        pool.wait_ge(rope_link.sem, rope_link.after(f - 1))
                    pool.tensor_tensor(heads4(xc), heads4(qkn), per_head(cs[:, 0]), ALU.mult
                                       ).then_inc(cosined.sem, 1)

                def mask(u):
                    pool.wait_ge(exp_ready.sem, exp_ready.after(b, u + 1))
                    apart(pool)
                    d = pT[:, u % 3, :, 0:P]
                    pool.affine_select(d, d, [[0, GRP], [1, P]], ALU.is_ge, 0.0, base=0,
                                       channel_multiplier=-1).then_inc(masked.sem, 1)

                if back and not b_cross:
                    for u in range(NU):
                        mask(u)
                if back and routes_last(b, b_cross):
                    scatter(b - 1)
                if not front:
                    scatter(b)

            over(step, pool.Fori)
            pool.wait_ge(scattered.sem, scattered.after(2 * B - 1))
            pool.wait_ge(table_ready, 3)
            for e in range(NE):
                pool.indirect_dma_start(
                    out=xs_dram, out_offset=bass.IndirectOffsetOnAxis(ap=cnti[:, 0, e:e + 1], axis=0),
                    in_=pay[:, 0, :], in_offset=None).then_inc(pads_scattered, 16)
            pool.wait_ge(pads_out, 32)
            pool.wait_ge(x2_out.sem, x2_out.after(2 * B - 1))

            def tile(f, b, fp):
                if b is None:
                    return
                pool.wait_ge(ye_link.sem, ye_link.after(b))
                if added.begun(b - 1):
                    pool.wait_ge(added.sem, added.after(b - 1))
                apart(pool)
                pool.indirect_dma_start(
                    out=acc_dram, out_offset=bass.IndirectOffsetOnAxis(ap=rowid[:, 1 - fp, 0:1], axis=0),
                    in_=ye[:, 1 - fp], in_offset=None, compute_op=ALU.add).then_inc(added.sem, 16)

            over_tiles(tile, pool.Fori)


def shape_constants():
    ident = np.eye(P, dtype=np.float32)
    later = np.triu(np.ones((P, P), np.float32), 1)
    cst = np.stack([ident, later * np.float32(MASKED), later], axis=1)
    small = np.zeros((P, 256), np.float32)
    small[:, 0:8] = np.arange(NE)
    small[:, 8:16] = np.arange(NE) * REGION
    small[:, 16] = np.arange(P)
    small[:, 17] = np.arange(P) + N
    small[:, 32:32 + TILES] = np.arange(TILES)
    small[:, 128:192] = np.tril(np.ones((NE, NE), np.float32)).reshape(-1)
    inv = (1.0 / np.float32(10000.0) ** (np.arange(0, D, 2, dtype=np.float32) / np.float32(D))).astype(np.float32)
    ang = np.arange(T, dtype=np.float32)[:, None] * inv
    ang = np.concatenate([ang, ang], 1)
    sign = np.concatenate([-np.ones(D // 2), np.ones(D // 2)]).astype(np.float32)
    rope = np.stack([np.cos(ang), np.sin(ang) * sign]).astype(np.float32)
    rope = rope.reshape(2, NT, P, 1, D).transpose(2, 0, 1, 3, 4)
    rope = np.concatenate([rope * np.float32(D ** -0.5), rope], axis=3)
    return cst, small, np.ascontiguousarray(rope)


def kernel(**inputs):
    import concourse.bacc as bacc
    from concourse.bass_utils import run_bass_kernel_spmd

    a = {k: np.asarray(v) for k, v in inputs.items()}

    def rows_of(w):
        return w.reshape(-1, P, w.shape[1]).transpose(1, 0, 2)

    def spread(v):
        return np.broadcast_to(v, (P,) + v.shape)

    def qk(q, k):
        return np.broadcast_to(np.stack([q, k]), (P, NT, 2, D))

    cst, small, rope = shape_constants()
    arrays = {
        "x": a["x"].reshape(N, E),
        "xT": a["x"].reshape(N, E).T,
        "ctxT": a["ctx_1024"].reshape(N, E).T,
        "wqk_self": rows_of(np.concatenate([a["L0_attn_Wq"].T, a["L0_attn_Wk"].T], axis=1)),
        "wv_self": rows_of(a["L0_attn_Wv"].T),
        "wo_self": rows_of(a["L0_attn_Wo"].T),
        "wq_x": rows_of(a["L0_xattn_Wq"]),
        "wk_x": rows_of(a["L0_xattn_Wk"]),
        "wv_x": rows_of(a["L0_xattn_Wv"]),
        "wo_x": rows_of(a["L0_xattn_Wo"]),
        "bo_self": spread(a["L0_attn_bo"]),
        "bo_x": spread(a["L0_xattn_bo"]),
        "gains": qk(a["L0_attn_qln_g"], a["L0_attn_kln_g"]),
        "shifts": qk(a["L0_attn_qln_b"], a["L0_attn_kln_b"]),
        "bq_x": spread(a["L0_xattn_bq"]),
        "bk_x": spread(a["L0_xattn_bk"]),
        "bv_x": spread(a["L0_xattn_bv"]),
        "rope": rope,
        "router": rows_of(a["L0_ffn_router_w"].T),
        "w1": a["L0_ffn_w1"].reshape(NE, F, KC, P).transpose(3, 2, 0, 1),
        "b1": spread(a["L0_ffn_b1"]),
        "w2": a["L0_ffn_w2"].reshape(NE, E, FC, P).transpose(3, 2, 0, 1),
        "b2": spread(a["L0_ffn_b2"]),
        "consts": cst,
        "tables": small,
    }
    arrays = {k: np.ascontiguousarray(v) for k, v in arrays.items()}
    nc = bacc.Bacc("TRN2", target_bir_lowering=False, num_devices=1)
    args = [nc.dram_tensor(k, v.shape, mybir.dt.from_np(v.dtype), kind="ExternalInput").ap()
            for k, v in arrays.items()]
    args.append(nc.dram_tensor("result", (N, E), F32, kind="ExternalOutput").ap())
    decoder_block(nc, *args)
    r = run_bass_kernel_spmd(nc, [arrays], core_ids=[0])
    return r.results[0]["result"].reshape(B, T, E)
```
